# Optimizing a Trainium2 kernel written in Bass

```python
import numpy as np
import jax
import jax.numpy as jnp

def _softmax(x, axis=-1):
    return jax.nn.softmax(x, axis=axis)

def _gelu(x):
    return jax.nn.gelu(x, approximate=True)

def _silu(x):
    return jax.nn.silu(x)

def _sigmoid(x):
    return jax.nn.sigmoid(x)

def _layernorm(x, axis=-1, eps=1e-05):
    m = jnp.mean(x, axis=axis, keepdims=True)
    v = jnp.var(x, axis=axis, keepdims=True)
    return (x - m) / jnp.sqrt(v + eps)

def _scatter_add(tgt, idx, src, axis=0):
    return tgt.at[idx].add(src)

def _segment_sum(src, seg, n):
    return jax.ops.segment_sum(src, seg, n)
kernel_name = 'mk_adaln_d2_jaxref_r8_c07bad'

def setup_inputs(seed: int=0):
    np.random.seed(seed)
    _w = jnp.asarray

    def _L0_attn_setup():
        import jax, jax.numpy as jnp
        import numpy as np
        HEADS = 4
        DIM_HEAD = 32
        EPS = 1e-05
        key = jax.random.key(seed)
        ks = jax.random.split(key, 6)
        b, n, dim = (8, 512, 128)
        hidden = HEADS * DIM_HEAD
        x = jax.random.normal(ks[0], (b, n, dim), dtype=jnp.float32)
        gamma = jnp.ones((1, 1, dim), dtype=jnp.float32)
        beta = jnp.zeros((1, 1, dim), dtype=jnp.float32)
        w_qkv = jax.random.normal(ks[1], (dim, hidden * 3), dtype=jnp.float32) / np.sqrt(dim)
        w_out = jax.random.normal(ks[2], (hidden, dim), dtype=jnp.float32) / np.sqrt(hidden)
        b_out = jnp.zeros((dim,), dtype=jnp.float32)
        return {'x': x, 'gamma': gamma, 'beta': beta, 'w_qkv': w_qkv, 'w_out': w_out, 'b_out': b_out}
    _L0_attn_in = _L0_attn_setup()

    def _L0_ffn_setup():
        import jax, jax.numpy as jnp
        import numpy as np
        E = 8
        TOP_K = 2
        H = 128
        F = 512
        LN_EPS = 1e-12
        key = jax.random.key(seed)
        ks = jax.random.split(key, 9)
        s = lambda k, shape, scale: jax.random.normal(k, shape, dtype=jnp.float32) * scale
        return {'hidden_states': s(ks[0], (4, 256, H), 1.0), 'Wr': s(ks[1], (E, H), 0.02), 'br': jnp.zeros((E,), jnp.float32), 'W1': s(ks[2], (E, F, H), 0.02), 'b1': jnp.zeros((E, F), jnp.float32), 'W2': s(ks[3], (E, H, F), 0.02), 'b2': jnp.zeros((E, H), jnp.float32), 'ln_w': jnp.ones((H,), jnp.float32), 'ln_b': jnp.zeros((H,), jnp.float32)}
    _L0_ffn_in = _L0_ffn_setup()
    _L0_c = _w((lambda *s: np.random.randn(*s).astype(np.float32) * 0.05)(8, 128))
    _L0_wmod = _w((lambda *s: np.random.randn(*s).astype(np.float32) * 0.05)(128, 6 * 128) * 128 ** (-0.5))

    def _L1_attn_setup():
        import jax, jax.numpy as jnp
        import numpy as np
        D = 128
        K_LOW1 = D // 4
        K_LOW2 = D // 4

        def mix_precision_matmul(x, w):
            d = x.shape[-1]
            w1 = w[:K_LOW1]
            wh = w[K_LOW1:d - K_LOW2]
            w2 = w[d - K_LOW2:]
            y1 = jnp.matmul(x[..., :K_LOW1].astype(jnp.float16), w1.astype(jnp.float16)).astype(jnp.float32)
            yh = jnp.matmul(x[..., K_LOW1:d - K_LOW2], wh)
            y2 = jnp.matmul(x[..., d - K_LOW2:].astype(jnp.float16), w2.astype(jnp.float16)).astype(jnp.float32)
            return y1 + yh + y2
        key = jax.random.key(seed)
        k1, k2, k3, k4 = jax.random.split(key, 4)
        B, N, d = (8, 256, D)
        x = jax.random.normal(k1, (B, N, d), dtype=jnp.float32)
        weight_qkv = jax.random.normal(k2, (d, 3 * d), dtype=jnp.float32) * d ** (-0.5)
        out_w = jax.random.normal(k3, (d, d), dtype=jnp.float32) * d ** (-0.5)
        out_b = jax.random.normal(k4, (d,), dtype=jnp.float32) * 0.01
        return {'x': x, 'weight_qkv': weight_qkv, 'out_w': out_w, 'out_b': out_b}
    _L1_attn_in = _L1_attn_setup()

    def _L1_ffn_setup():
        import jax, jax.numpy as jnp
        import numpy as np
        D_MODEL = 128
        HIDDEN = 512
        NUM_EXPERTS = 8
        TOP_K = 2
        NUM_SHARED = 2

        def _gelu(x):
            return jax.nn.gelu(x, approximate=False)
        key = jax.random.key(seed)
        ks = jax.random.split(key, 12)
        s = 0.02
        return {'x': jax.random.normal(ks[0], (2, 256, D_MODEL), dtype=jnp.float32), 'rW': jax.random.normal(ks[1], (D_MODEL, NUM_EXPERTS), dtype=jnp.float32) * s, 'rb': jnp.zeros((NUM_EXPERTS,), dtype=jnp.float32), 'W1': jax.random.normal(ks[2], (NUM_EXPERTS, D_MODEL, HIDDEN), dtype=jnp.float32) * s, 'b1': jnp.zeros((NUM_EXPERTS, HIDDEN), dtype=jnp.float32), 'W2': jax.random.normal(ks[3], (NUM_EXPERTS, HIDDEN, D_MODEL), dtype=jnp.float32) * s, 'b2': jnp.zeros((NUM_EXPERTS, D_MODEL), dtype=jnp.float32), 'sW1': jax.random.normal(ks[4], (NUM_SHARED, D_MODEL, HIDDEN), dtype=jnp.float32) * s, 'sb1': jnp.zeros((NUM_SHARED, HIDDEN), dtype=jnp.float32), 'sW2': jax.random.normal(ks[5], (NUM_SHARED, HIDDEN, D_MODEL), dtype=jnp.float32) * s, 'sb2': jnp.zeros((NUM_SHARED, D_MODEL), dtype=jnp.float32)}
    _L1_ffn_in = _L1_ffn_setup()
    _L1_c = _w((lambda *s: np.random.randn(*s).astype(np.float32) * 0.05)(8, 128))
    _L1_wmod = _w((lambda *s: np.random.randn(*s).astype(np.float32) * 0.05)(128, 6 * 128) * 128 ** (-0.5))
    _d = {'L0_attn_x': _L0_attn_in['x'], 'L0_attn_gamma': _L0_attn_in['gamma'], 'L0_attn_beta': _L0_attn_in['beta'], 'L0_attn_w_qkv': _L0_attn_in['w_qkv'], 'L0_attn_w_out': _L0_attn_in['w_out'], 'L0_attn_b_out': _L0_attn_in['b_out'], 'L0_ffn_Wr': _L0_ffn_in['Wr'], 'L0_ffn_br': _L0_ffn_in['br'], 'L0_ffn_W1': _L0_ffn_in['W1'], 'L0_ffn_b1': _L0_ffn_in['b1'], 'L0_ffn_W2': _L0_ffn_in['W2'], 'L0_ffn_b2': _L0_ffn_in['b2'], 'L0_ffn_ln_w': _L0_ffn_in['ln_w'], 'L0_ffn_ln_b': _L0_ffn_in['ln_b'], 'L0_c': _L0_c, 'L0_wmod': _L0_wmod, 'L1_attn_weight_qkv': _L1_attn_in['weight_qkv'], 'L1_attn_out_w': _L1_attn_in['out_w'], 'L1_attn_out_b': _L1_attn_in['out_b'], 'L1_ffn_rW': _L1_ffn_in['rW'], 'L1_ffn_rb': _L1_ffn_in['rb'], 'L1_ffn_W1': _L1_ffn_in['W1'], 'L1_ffn_b1': _L1_ffn_in['b1'], 'L1_ffn_W2': _L1_ffn_in['W2'], 'L1_ffn_b2': _L1_ffn_in['b2'], 'L1_ffn_sW1': _L1_ffn_in['sW1'], 'L1_ffn_sb1': _L1_ffn_in['sb1'], 'L1_ffn_sW2': _L1_ffn_in['sW2'], 'L1_ffn_sb2': _L1_ffn_in['sb2'], 'L1_c': _L1_c, 'L1_wmod': _L1_wmod}
    _x0 = _d['L0_attn_x']
    _d['L0_attn_x'] = jax.random.normal(jax.random.fold_in(jax.random.key(seed), 1), (8, 256, 128), dtype=_x0.dtype)
    del _x0
    return _d

def reference(L0_attn_x, L0_attn_gamma, L0_attn_beta, L0_attn_w_qkv, L0_attn_w_out, L0_attn_b_out, L0_ffn_Wr, L0_ffn_br, L0_ffn_W1, L0_ffn_b1, L0_ffn_W2, L0_ffn_b2, L0_ffn_ln_w, L0_ffn_ln_b, L0_c, L0_wmod, L1_attn_weight_qkv, L1_attn_out_w, L1_attn_out_b, L1_ffn_rW, L1_ffn_rb, L1_ffn_W1, L1_ffn_b1, L1_ffn_W2, L1_ffn_b2, L1_ffn_sW1, L1_ffn_sb1, L1_ffn_sW2, L1_ffn_sb2, L1_c, L1_wmod):

    def _L0_attn_ref(x, gamma, beta, w_qkv, w_out, b_out):
        import jax, jax.numpy as jnp
        import numpy as np
        HEADS = 4
        DIM_HEAD = 32
        EPS = 1e-05
        b, n, dim = x.shape
        mean = jnp.mean(x, axis=2, keepdims=True)
        var = jnp.var(x, axis=2, keepdims=True)
        xn = (x - mean) / jnp.sqrt(var + EPS) * gamma + beta
        qkv = jnp.einsum('bnc,ck->bnk', xn, w_qkv)
        q, k, v = jnp.split(qkv, 3, axis=2)

        def to_heads(t):
            return t.reshape(b, n, HEADS, DIM_HEAD)
        q, k, v = (to_heads(q), to_heads(k), to_heads(v))
        q = q * DIM_HEAD ** (-0.5)
        k = jax.nn.softmax(k, axis=1)
        context = jnp.einsum('bnhd,bnhe->bhde', k, v)
        out = jnp.einsum('bhde,bnhd->bnhe', context, q)
        out = out.reshape(b, n, HEADS * DIM_HEAD)
        out = jnp.einsum('bnk,kc->bnc', out, w_out) + b_out
        return out + x

    def _L0_ffn_ref(hidden_states, Wr, br, W1, b1, W2, b2, ln_w, ln_b):
        import jax, jax.numpy as jnp
        import numpy as np
        E = 8
        TOP_K = 2
        H = 128
        F = 512
        LN_EPS = 1e-12
        bsz, seqlen, h = hidden_states.shape
        x = hidden_states.reshape(-1, h)
        logits = x @ Wr.T + br
        topk_vals, topk_idx = jax.lax.top_k(logits, TOP_K)
        topk_w = jax.nn.softmax(topk_vals, axis=-1)
        out = jnp.zeros_like(x)
        for e in range(E):
            cw = jnp.sum(topk_w * (topk_idx == e), axis=-1)
            y = jax.nn.gelu(x @ W1[e].T + b1[e], approximate=False) @ W2[e].T + b2[e]
            out = out + cw[:, None] * y
        z = out + x
        mu = jnp.mean(z, axis=-1, keepdims=True)
        var = jnp.mean(jnp.square(z - mu), axis=-1, keepdims=True)
        z = (z - mu) * jax.lax.rsqrt(var + LN_EPS) * ln_w + ln_b
        return z.reshape(bsz, seqlen, h)

    def _L1_attn_ref(x, weight_qkv, out_w, out_b):
        import jax, jax.numpy as jnp
        import numpy as np
        D = 128
        K_LOW1 = D // 4
        K_LOW2 = D // 4

        def mix_precision_matmul(x, w):
            d = x.shape[-1]
            w1 = w[:K_LOW1]
            wh = w[K_LOW1:d - K_LOW2]
            w2 = w[d - K_LOW2:]
            y1 = jnp.matmul(x[..., :K_LOW1].astype(jnp.float16), w1.astype(jnp.float16)).astype(jnp.float32)
            yh = jnp.matmul(x[..., K_LOW1:d - K_LOW2], wh)
            y2 = jnp.matmul(x[..., d - K_LOW2:].astype(jnp.float16), w2.astype(jnp.float16)).astype(jnp.float32)
            return y1 + yh + y2
        d = x.shape[-1]
        qkv = mix_precision_matmul(x, weight_qkv)
        q, k, v = jnp.split(qkv, 3, axis=-1)
        q = q / jnp.sqrt(jnp.asarray(d, dtype=q.dtype))
        qk = jnp.einsum('bqd,bkd->bqk', q, k)
        s = jax.nn.softmax(qk, axis=-1)
        y = jnp.einsum('bqk,bkd->bqd', s, v)
        return jnp.matmul(y, out_w.T) + out_b

    def _L1_ffn_ref(x, rW, rb, W1, b1, W2, b2, sW1, sb1, sW2, sb2):
        import jax, jax.numpy as jnp
        import numpy as np
        D_MODEL = 128
        HIDDEN = 512
        NUM_EXPERTS = 8
        TOP_K = 2
        NUM_SHARED = 2

        def _gelu(x):
            return jax.nn.gelu(x, approximate=False)
        B, L, D = x.shape
        xf = x.reshape(-1, D)
        sh = _gelu(jnp.einsum('td,sdh->sth', xf, sW1) + sb1[:, None, :])
        shared = jnp.einsum('sth,shd->std', sh, sW2) + sb2[:, None, :]
        shared = shared.mean(axis=0)
        gates = xf @ rW + rb
        topk_vals, topk_idx = jax.lax.top_k(gates, TOP_K)
        topk_probs = jax.nn.softmax(topk_vals, axis=-1)
        onehot = topk_idx[:, :, None] == jnp.arange(NUM_EXPERTS)[None, None, :]
        w = jnp.sum(topk_probs[:, :, None] * onehot, axis=1)
        h = _gelu(jnp.einsum('td,edh->eth', xf, W1) + b1[:, None, :])
        y = jnp.einsum('eth,ehd->etd', h, W2) + b2[:, None, :]
        moe = jnp.einsum('te,etd->td', w, y)
        return (shared + moe).reshape(B, L, D)
    x = L0_attn_x
    mod = (_silu(L0_c) @ L0_wmod).reshape(L0_c.shape[0], 6, 1, -1)
    sa, ca, ga, sb, cb, gb = (mod[:, 0], mod[:, 1], mod[:, 2], mod[:, 3], mod[:, 4], mod[:, 5])
    ga = (2 * (ga >= 0) - 1) * jnp.maximum(jnp.abs(ga), 0.25)
    gb = (2 * (gb >= 0) - 1) * jnp.maximum(jnp.abs(gb), 0.25)
    h = _layernorm(x, axis=-1) * (1 + ca) + sa
    x = x + ga * _L0_attn_ref(h, L0_attn_gamma, L0_attn_beta, L0_attn_w_qkv, L0_attn_w_out, L0_attn_b_out)
    h = _layernorm(x, axis=-1) * (1 + cb) + sb
    x = x + gb * _L0_ffn_ref(h, L0_ffn_Wr, L0_ffn_br, L0_ffn_W1, L0_ffn_b1, L0_ffn_W2, L0_ffn_b2, L0_ffn_ln_w, L0_ffn_ln_b)
    mod = (_silu(L1_c) @ L1_wmod).reshape(L1_c.shape[0], 6, 1, -1)
    sa, ca, ga, sb, cb, gb = (mod[:, 0], mod[:, 1], mod[:, 2], mod[:, 3], mod[:, 4], mod[:, 5])
    ga = (2 * (ga >= 0) - 1) * jnp.maximum(jnp.abs(ga), 0.25)
    gb = (2 * (gb >= 0) - 1) * jnp.maximum(jnp.abs(gb), 0.25)
    h = _layernorm(x, axis=-1) * (1 + ca) + sa
    x = x + ga * _L1_attn_ref(h, L1_attn_weight_qkv, L1_attn_out_w, L1_attn_out_b)
    h = _layernorm(x, axis=-1) * (1 + cb) + sb
    x = x + gb * _L1_ffn_ref(h, L1_ffn_rW, L1_ffn_rb, L1_ffn_W1, L1_ffn_b1, L1_ffn_W2, L1_ffn_b2, L1_ffn_sW1, L1_ffn_sb1, L1_ffn_sW2, L1_ffn_sb2)
    return x

_drawn_inputs = setup_inputs


def setup_inputs(seed=0):
    import zlib

    import numpy as np

    out = dict(_drawn_inputs(seed))
    spreads = {'L0_attn_gamma': (1.0, 0.6),
     'L0_attn_beta': (0.0, 0.348),
     'L0_attn_b_out': (0.0, 0.339),
     'L0_ffn_br': (0.0, 0.474),
     'L0_ffn_b1': (0.0, 0.8),
     'L0_ffn_b2': (0.0, 0.482),
     'L0_ffn_ln_w': (1.0, 0.2),
     'L0_ffn_ln_b': (0.0, 0.344),
     'L1_ffn_rb': (0.0, 0.613),
     'L1_ffn_b1': (0.0, 0.8),
     'L1_ffn_b2': (0.0, 0.465),
     'L1_ffn_sb1': (0.0, 0.8),
     'L1_ffn_sb2': (0.0, 0.462)}
    factors = {'L0_ffn_Wr': 3.605,
     'L0_ffn_W1': 6.002,
     'L0_ffn_W2': 5.497,
     'L1_attn_out_b': 8.0,
     'L1_ffn_rW': 3.387,
     'L1_ffn_W1': 6.331,
     'L1_ffn_W2': 5.711,
     'L1_ffn_sW1': 6.335,
     'L1_ffn_sW2': 5.701}
    for name, (base, spread) in spreads.items():
        noise = np.random.default_rng([zlib.crc32(name.encode()), seed]).standard_normal(out[name].shape)
        drawn = base * np.exp(spread * noise) if base else spread * noise
        out[name] = jnp.asarray(drawn.astype(out[name].dtype))
    for name, factor in factors.items():
        out[name] = (out[name] * factor).astype(out[name].dtype)
    return out
```

```python
from contextlib import ExitStack

import concourse.bass as bass
from concourse import mybir

F32 = mybir.dt.float32
F16 = mybir.dt.float16
U32 = mybir.dt.uint32
ALU = mybir.AluOpType
ACT = mybir.ActivationFunctionType
AX_X = mybir.AxisListType.X

P = 128
D = 128
B = 8
N = 256
GB = 2
G = B // GB
T = GB * N
TT = T // P
F = 512
FC = F // P
NE = 8
NSH = 2
EXPERTS = (NE, NE + NSH)
DH = 32
BAND = D // 4
WSCALE = 64.0
LAG = 3
HEAD = 5
RING = 8
GRING = 4
STG = 3
PER_LOOP = STG
LN_EPS, LN_EPS_FFN = 1e-5, 1e-12
ROWS = ("ca1", "sa", "ga", "gab", "gblw", "gblb", "ga_1", "gab_1")
POOL_CHUNKS = (1, 3)
FIRST = 1
CREDITS = {"hT": FIRST, "att": FIRST, "z_turned": FIRST, "z_read": FIRST, "cwb_done": FIRST,
           "gelu_done": 2, "w2_done": RING, "y_used": 2, "add_done": 2,
           "lo_vector": FC - len(POOL_CHUNKS), "lo_pool": len(POOL_CHUNKS)}


def build(nc, dram, out):
    with ExitStack() as ctx:
        def sb(name, shape, dt=F32):
            return ctx.enter_context(nc.sbuf_tensor(name, shape, dt))

        def ps(name):
            return ctx.enter_context(nc.psum_tensor(name, [P, T], F32))

        sems = {}

        def sem(name):
            if name not in sems:
                sems[name] = ctx.enter_context(nc.semaphore(name))
            return sems[name]

        X = sb("X", [P, B * N // P, D])
        w_hi = [sb(f"w_hi{l}", [P, EXPERTS[l], 2, F], F16) for l in range(2)]
        w_lo = [sb(f"w_lo{l}", [P, EXPERTS[l], 2, F], F16) for l in range(2)]
        w_stage = sb("w_stage", [P, STG, 2, F])
        rows = sb("rows", [P, B, len(ROWS), D])
        cols = sb("cols", [P, 2, 6, B])
        vecs = sb("vecs", [P, 4 + FC * sum(EXPERTS)])
        bvec = sb("bvec", [P, 4 * D + 2 * NE])
        att0 = sb("att0", [P, 4 * D + 2 * NE])
        att1 = sb("att1", [P, 4 * D])
        wmid = sb("wmid", [P, 3 * D])
        wband = sb("wband", [P, 2, 3 * D], F16)
        b2 = sb("b2", [P, 2, D])
        b2_hi = sb("b2_hi", [P, 2, D], F16)
        b2_lo = sb("b2_lo", [P, 2, D], F16)
        sb2 = sb("sb2", [P, 2])
        ident = sb("ident", [P, P])
        ident16 = sb("ident16", [P, P], F16)
        spread = sb("spread", [P, NE, P], F16)
        heads = sb("heads", [P, D])
        iota8 = sb("iota8", [P, NE])
        neghalf = sb("neghalf", [P, TT])
        eps = sb("eps", [P, 2, TT])
        carrier = sb("carrier", [P, 1])
        sig = sb("sig", [P, 2 * B])
        silu = sb("silu", [P, 2 * B])
        signc = sb("signc", [P, B])
        st6 = sb("st6", [P, TT, 6])
        mv = sb("mv", [P, TT, 2])
        veps = sb("veps", [P, TT])
        rstd = sb("rstd", [P, TT])
        hn = sb("hn", [P, TT, D])
        hnT = sb("hnT", [P, T])
        h16 = sb("h16", [P, T], F16)
        v_tok = sb("v_tok", [P, T])
        negmax = sb("negmax", [P, TT])
        esum = sb("esum", [P, TT])
        rsum = sb("rsum", [P, TT])
        rsum_s = sb("rsum_s", [P, TT])
        low = sb("low", [P, 2, T], F16)
        yT = sb("yT", [P, T])
        att = hn
        shared = sb("shared", [P, 2 * TT * N])
        qk = sb("qk", [P, 2 * T])

        def view(mem, start, shape, parts=P):
            size = 1
            for n in shape:
                size *= n
            names = " ".join("xyz"[:len(shape)])
            a = mem[0:parts, start:start + size]
            return a if len(shape) == 1 else a.rearrange(f"p ({names}) -> p {names}", **dict(zip("xyz", shape)))

        modin = view(shared, 0, [2 * B + 12 * D])
        rowc = view(qk, 0, [len(ROWS), D], B)
        eT, e_tok = view(shared, 0, [T]), view(shared, T, [T])
        h_tok = view(shared, 2 * T, [TT, D])
        ctxm, ctxw = (view(shared, 3 * T + n * GB * D, [GB, D]) for n in range(2))
        qctx = view(qk, 0, [GB, D])
        qT, kT = view(qk, 0, [T]), view(qk, T, [T])
        prob = view(shared, 0, [TT, N])
        probT = view(shared, TT * N, [GB, 2, N])
        hT = sb("hT", [P, T])
        x_hi = sb("x_hi", [P, T], F16)
        x_lo = sb("x_lo", [P, T], F16)
        g32 = sb("g32", [P, GRING, T])
        g_flat = g32[:, :, :].rearrange("p g t -> p (g t)")
        modr = view(g_flat, 0, [2, 6, D], B)
        signr = view(g_flat, 12 * D, [3, D], B)
        g_hi = sb("g_hi", [P, RING, T], F16)
        g_lo = sb("g_lo", [P, RING, T], F16)
        cwb = sb("cwb", [P, 2, T])
        yw = sb("yw", [P, 2, T])
        magr = view(yw[:, :, :].rearrange("p k t -> p (k t)"), 0, [3, D], B)
        acc = sb("acc", [P, T])
        lg = sb("lg", [P, TT, NE])
        top = sb("top", [P, TT, 8])
        topi = sb("topi", [P, TT, 8], U32)
        topf = sb("topf", [P, TT, 8])
        gap = sb("gap", [P, TT])
        th = sb("th", [P, TT])
        pr = sb("pr", [P, 2, TT])
        pick = sb("pick", [P, 2, TT, NE])
        cw = sb("cw", [P, TT, NE])
        cw_parts = sb("cw_parts", [P, TT, P], F16)
        cwT = sb("cwT", [P, T], F16)
        zst6 = sb("zst6", [P, TT, 6])
        zmv = sb("zmv", [P, TT, 2])
        zveps = sb("zveps", [P, TT])
        zrstd = sb("zrstd", [P, TT])
        zn = sb("zn", [P, TT, D])
        pH = [ps(f"pH{i}") for i in range(2)]
        pY = [ps(f"pY{i}") for i in range(2)]
        pC = ps("pC")
        pZ = ps("pZ")
        pA = [ps(f"pA{i}") for i in range(2)]
        pC16 = pC[:, 0:T // 2].bitcast(F16)

        rows_dram = nc.dram_tensor("rows_dram", [B, len(ROWS) * D], F32, kind="Internal").ap()

        wk, wv, wout, wqT = (att0[:, n * D:(n + 1) * D] for n in range(4))
        wr = [att0[:, 4 * D + l * NE:4 * D + (l + 1) * NE] for l in range(2)]
        outwT = att1[:, 3 * D:4 * D]
        gamma, beta = vecs[:, 0:1], vecs[:, 1:2]
        br = [bvec[:, 4 * D + l * NE:4 * D + (l + 1) * NE] for l in range(2)]
        wmod = [modin[:, 2 * B + l * 6 * D:2 * B + (l + 1) * 6 * D] for l in range(2)]

        def at(start, n=1):
            return slice(start, start + n) if isinstance(start, int) else bass.ds(start, n)

        def xg(f):
            return X[:, at(f[1] * TT, TT), :]

        def xt(f, t):
            return X[:, at(f[1] * TT + t), :]

        def row(f, name, t):
            return rows[:, at(f[1] * GB + t * GB // TT), ROWS.index(name), :]

        def rowg(f, name):
            r = rows[:, at(f[1] * GB, GB), ROWS.index(name), :]
            return r.unsqueeze(2).broadcast_to([P, GB, TT // GB, D])

        def by_batch(a):
            return a.rearrange("p (b t) d -> p b t d", b=GB)

        def col(f, kind, j):
            return cols[:, f[0], kind, at(f[1] * GB + j)]

        def bt(a, j):
            return a[:, j * N:(j + 1) * N]

        def tc(a, t):
            return a[:, t * P:(t + 1) * P]

        def b1(f, q):
            n = 4 + FC * (EXPERTS[0] if f[0] else 0) + q
            return vecs[:, n:n + 1]

        def nth(f, done=1):
            return (G if f[0] else 0) + f[1] + done

        def over(per, f, k):
            return (G * per[0] if f[0] else 0) + per[f[0]] * f[1] + k

        def chunks(f, k):
            return over((FC * EXPERTS[0], FC * EXPERTS[1]), f, k)

        def experts(f, k):
            return over(EXPERTS, f, k)

        def low_part(f, q):
            e, c = divmod(q, FC)
            mine = [n for n in range(FC) if (n in POOL_CHUNKS) == (c in POOL_CHUNKS)]
            name = "lo_pool" if c in POOL_CHUNKS else "lo_vector"
            return sem(name), over((len(mine) * EXPERTS[0], len(mine) * EXPERTS[1]), f, len(mine) * e + mine.index(c) + 1)

        def before(f, q, prev, back):
            if q >= back:
                return (f, q - back) if f else None
            return (prev, FC * EXPERTS[prev[0]] + q - back) if prev else None

        def expert_at(f, q, prev, back):
            was = before(f, q, prev, back)
            return (was[0], was[1] // FC) if was and was[1] % FC == 0 and was[1] >= 0 else None

        def is_last_of_0(f):
            return f is not None and f[0] == 0 and isinstance(f[1], int)

        def whole_program(eng, attention, slot, steps, post, split_x):
            def rest(f, a, nxt=None):
                for q in range(HEAD, FC * EXPERTS[f[0]]):
                    slot(f, q, None if q >= 3 * FC else f and None)
                    for when, step in (steps[a[0]] if a else ()):
                        if when == q:
                            step(a, f)
                if a:
                    split_x(a, f)

            def head(f, prev):
                for q in range(HEAD):
                    slot(f, q, prev)
                    if prev:
                        post(prev, q)

            attention()
            split_x((0, 0), None)
            head((0, 0), None)
            with eng.Fori(0, G - 1) as i:
                rest((0, i), (0, i + 1))
                head((0, i + 1), (0, i))
            rest((0, G - 1), (1, 0))
            head((1, 0), (0, G - 1))
            with eng.Fori(0, G - 1) as i:
                rest((1, i), (1, i + 1))
                head((1, i + 1), (1, i))
            rest((1, G - 1), None)
            head(None, (1, G - 1))

        def nothing(*_):
            pass

        block = ctx.enter_context(nc.Block())

        @block.sync
        def _(sp):
            def load_w(n):
                if n >= STG:
                    sp.wait_ge(sem("w_hi_done"), n - STG + 1)
                    sp.wait_ge(sem("w_lo_done"), n - STG + 1)
                src = dram["w_0"][n] if n < NE else dram["w_1"][n - NE]
                sp.dma_start(w_stage[:, n % STG, :, :], src).then_inc(sem(f"w_in{n % STG}"), 16)

            sp.dma_start(modin, dram["modin"]).then_inc(sem("modin_in"), 16)
            sp.dma_start(X[:, 0:TT, :], dram["x"][:, 0:TT, :]).then_inc(sem("x_in0"), 16)
            sp.dma_start(bvec[:, :], dram["bvec"].partition_broadcast(P)).then_inc(sem("bvec_in"), 16)
            sp.dma_start(vecs[:, :], dram["vecs"]).then_inc(sem("vecs_in"), 16)
            sp.dma_start(att0[:, :], dram["att0"]).then_inc(sem("att0_in"), 16)
            sp.wait_ge(sem("b2_zero"), 1)
            sp.dma_start(b2[0:NE, :, :], dram["b2"]).then_inc(sem("b2_in"), 16)
            sp.dma_start(b2[NE:2 * NE, :, :], dram["b2"]).then_inc(sem("b2_in"), 16)
            for n in range(STG):
                load_w(n)
            sp.wait_ge(sem("rows_made"), 1)
            sp.dma_start(rows_dram, rowc[:, :, :].rearrange("b r d -> b (r d)")).then_inc(sem("rows_out"), 16)
            sp.wait_ge(sem("rows_out"), 16)
            for g in range(G):
                sp.dma_start(rows[:, g * GB:(g + 1) * GB, :, :].rearrange("p b r d -> p b (r d)"),
                             rows_dram[g * GB:(g + 1) * GB, :].partition_broadcast(P)
                             ).then_inc(sem("rows_in0" if g == 0 else "rows_in1"), 16)
            for n in range(STG, NE):
                load_w(n)
            sp.dma_start(X[:, TT:, :], dram["x"][:, TT:, :]).then_inc(sem("x_in1"), 16)
            sp.dma_start(att1[:, :], dram["att1"]).then_inc(sem("att1_in"), 16)
            for n in range(NE, sum(EXPERTS)):
                load_w(n)
            with sp.Fori(0, G) as g:
                sp.wait_ge(sem("z_read"), g + (G + 1) + FIRST)
                sp.dma_start(out[:, bass.ds(g * TT, TT), :], X[:, bass.ds(g * TT, TT), :]).then_inc(sem("out_done"), 16)
            sp.wait_ge(sem("out_done"), 16 * G)

        @block.tensor
        def _(pe):
            def mm(o, w, x, start=True, stop=True):
                return nc.tensor.matmul(o, w, x, start=start, stop=stop)

            def transposes(o, src, done):
                for t in range(TT):
                    last = nc.tensor.transpose(tc(o, t), src(t), ident[:, :])
                last.then_inc(done, 1)

            def slot(f, q, prev):
                was = before(f, q, prev, LAG)
                if was:
                    g, r = was
                    e, c = divmod(r, FC)
                    pe.wait_ge(*low_wait(g, r))
                    if c == 0:
                        pe.wait_ge(sem("y_used"), experts(g, e + 1))
                    y, w = pY[e % 2][:, :], slice(c * P, (c + 1) * P)
                    mm(y, w_hi[g[0]][:, e, 1, w], g_hi[:, r % RING, :], start=(c == 0), stop=False)
                    mm(y, w_lo[g[0]][:, e, 1, w], g_hi[:, r % RING, :], start=False, stop=False)
                    mm(y, w_hi[g[0]][:, e, 1, w], g_lo[:, r % RING, :], start=False,
                       stop=(c == FC - 1)).then_inc(sem("w2_done"), 1)
                if not f:
                    return
                e, c = divmod(q, FC)
                if q == 0:
                    pe.wait_ge(sem("x_split"), nth(f))
                if c == 0:
                    n = e + 1 + (EXPERTS[0] if f[0] else 0)
                    pe.wait_ge(sem("w_hi_done"), n)
                    pe.wait_ge(sem("w_lo_done"), n)
                pe.wait_ge(sem("gelu_done"), chunks(f, q + 1))
                h, w = pH[q % 2][:, :], slice(c * P, (c + 1) * P)
                mm(h, w_hi[f[0]][:, e, 0, w], x_hi[:, :], stop=False)
                mm(h, w_lo[f[0]][:, e, 0, w], x_hi[:, :], start=False, stop=False)
                mm(h, w_hi[f[0]][:, e, 0, w], x_lo[:, :], start=False).then_inc(sem("hid_ready"), 1)
                if q == 0:
                    pe.wait_ge(sem("hT"), nth(f) + FIRST)
                    pe.wait_ge(sem("cwb_done"), over((NE, NE), f, 0) + FIRST)
                    for t in range(TT):
                        last = mm(pC[:, t * NE:(t + 1) * NE], tc(hT, t), wr[f[0]])
                    last.then_inc(sem("logits"), 1)
                if q == 6:
                    pe.wait_ge(sem("cw_parts"), nth(f))
                    for t in range(TT):
                        last = nc.tensor.transpose(tc(pC16, t), cw_parts[:, t, :], ident16[:, :])
                    last.then_inc(sem("cw_turned"), 1)
                if q == 7:
                    pe.wait_ge(sem("cwT"), nth(f))
                    pe.wait_ge(sem("z_read"), nth(f, 0) + FIRST)
                    mm(pZ[:, :], b2_hi[:, f[0], :], cwT[:, :], stop=False)
                    mm(pZ[:, :], b2_lo[:, f[0], :], cwT[:, :], start=False).then_inc(sem("b2_term"), 1)
                e = {7: 0, 8: 1}.get(q, (q - 3) // FC if q >= 11 and q % FC == 3 else None)
                if e is not None and e < NE:
                    pe.wait_ge(sem("cwb_done"), over((NE, NE), f, e) + FIRST)
                    mm(pC[:, :], spread[:, e, :], cwT[:, :]).then_inc(sem("cwb_ready"), 1)

            def low_wait(f, q):
                s, k = low_part(f, q)
                return s, k + CREDITS["lo_pool" if q % FC in POOL_CHUNKS else "lo_vector"]

            def post(f, q):
                if q == 3 + f[0]:
                    if f[0]:
                        pe.wait_ge(sem("acc_gated"), f[1] + 1)
                    else:
                        pe.wait_ge(sem("add_done"), experts(f, NE) + CREDITS["add_done"])
                    transposes(pZ, lambda t: tc(acc, t), sem("z_turned"))

            def turn_hn(a, f):
                pe.wait_ge(sem("hn"), nth(a))
                pe.wait_ge(sem("hT"), nth(a, 0) + FIRST)
                transposes(pA[0], lambda t: hn[:, t, :], sem("hn_turned"))

            def keys(a, f):
                if f is None:
                    pe.wait_ge(sem("att0_in"), 16)
                pe.wait_ge(sem("hnT"), nth(a))
                pe.wait_ge(sem("att"), nth(a, 0) + FIRST)
                mm(pA[1][:, :], wk, hnT[:, :]).then_inc(sem("k_ready"), 1)

            def values(a, f):
                for t in range(TT):
                    last = mm(tc(pA[0], t), tc(hnT, t), wv)
                last.then_inc(sem("v_ready"), 1)

            def turn_keys(a, f):
                pe.wait_ge(sem("exp_done"), nth(a))
                transposes(pA[1], lambda t: tc(eT, t), sem("e_turned"))

            def context(a, f):
                pe.wait_ge(sem("e_tok"), nth(a))
                pe.wait_ge(sem("v_tok"), nth(a))
                for b in range(GB):
                    for t in range(TT // GB):
                        n = b * TT // GB + t
                        last = mm(tc(pA[0], b), tc(v_tok, n), tc(e_tok, n), start=(t == 0), stop=(t == TT // GB - 1))
                last.then_inc(sem("ctx_ready"), 1)

            def context_out(a, f):
                pe.wait_ge(sem("ctxm"), nth(a))
                for b in range(GB):
                    last = mm(tc(pA[1], b), ctxm[:, b, :], wout)
                last.then_inc(sem("ctxw_ready"), 1)

            def query_context(a, f):
                pe.wait_ge(sem("ctxw"), nth(a))
                mm(pA[0][:, 0:GB * D], wqT, ctxw[:, :, :].rearrange("p b d -> p (b d)")).then_inc(sem("qctx_ready"), 1)

            def project0(a, f):
                pe.wait_ge(sem("qctx"), nth(a))
                for t in range(TT):
                    last = mm(tc(pA[1], t), tc(hnT, t), qctx[:, t * GB // TT, :])
                last.then_inc(sem("proj_ready"), 1)

            def turn_x2(a, f):
                pe.wait_ge(sem("xn2"), nth(a))
                transposes(pA[0], lambda t: hn[:, t, :], sem("xn2_turned"))

            def bands(n):
                def step(a, f):
                    if n == 0:
                        pe.wait_ge(sem("bands_made"), 1)
                        pe.wait_ge(sem("h16"), a[1] + 1)
                        pe.wait_ge(sem("att"), nth(a, 0) + FIRST)
                    else:
                        pe.wait_ge(sem("q_done" if n == 1 else "k_done"), a[1] + 1)
                    w = slice(n * D, (n + 1) * D)
                    for k in range(2):
                        if n < 2:
                            last = mm(pA[k][:, :], wband[:, k, w], h16[:, :])
                        else:
                            for t in range(TT):
                                last = mm(tc(pA[k], t), tc(h16, t), wband[:, k, w])
                    last.then_inc(sem("bands_ready"), 1)
                return step

            def band_sum(n):
                def step(a, f):
                    pe.wait_ge(sem("bands"), a[1] * 3 + n + 1)
                    w = slice(n * D, (n + 1) * D)
                    if n < 2:
                        mm(pA[0][:, :], wmid[:, w], hnT[:, :], stop=False)
                        mm(pA[0][:, :], ident16[:, :], low[:, 0, :], start=False, stop=False)
                        last = mm(pA[0][:, :], ident16[:, :], low[:, 1, :], start=False)
                    else:
                        for t in range(TT):
                            mm(tc(pA[0], t), tc(hnT, t), wmid[:, w], stop=False)
                            mm(tc(pA[0], t), ident16[:, :], tc(low[:, 0, :], t), start=False, stop=False)
                            last = mm(tc(pA[0], t), ident16[:, :], tc(low[:, 1, :], t), start=False)
                    last.then_inc(sem("sum_ready"), 1)
                return step

            def scores(a, f):
                pe.wait_ge(sem("v_tok"), nth(a))
                for t in range(TT):
                    b, j = divmod(t, TT // GB)
                    last = mm(bt(pA[b], j), tc(qT, t), bt(kT, b))
                last.then_inc(sem("scores"), 1)

            def turn_prob(a, f):
                pe.wait_ge(sem("exp_done"), nth(a))
                for b in range(GB):
                    for k in range(2):
                        for j in range(2):
                            last = nc.tensor.transpose(tc(pA[b], 2 * k + j), tc(prob[:, 2 * b + j, :], k), ident[:, :])
                last.then_inc(sem("prob_turned"), 1)

            def mix(a, f):
                pe.wait_ge(sem("probT_s"), a[1] + 1)
                pe.wait_ge(sem("probT_v"), a[1] + 1)
                for b in range(GB):
                    for k in range(2):
                        last = mm(bt(pA[0], b), tc(v_tok, 2 * b + k), probT[:, b, k, :], start=(k == 0), stop=(k == 1))
                last.then_inc(sem("mix_ready"), 1)

            def project1(a, f):
                pe.wait_ge(sem("yT"), a[1] + 1)
                for t in range(TT):
                    last = mm(tc(pA[1], t), tc(yT, t), outwT)
                last.then_inc(sem("proj_ready"), 1)

            steps = [
                [(9, turn_hn), (11, keys), (12, values), (13, turn_keys), (15, context), (17, context_out),
                 (19, query_context), (21, project0), (26, turn_x2)],
                [(7, turn_hn), (8, bands(0)), (9, band_sum(0)), (10, bands(1)), (11, band_sum(1)), (12, bands(2)),
                 (13, band_sum(2)), (15, scores), (17, turn_prob), (19, mix), (21, project1), (26, turn_x2)]]

            def attention():
                pe.wait_ge(sem("modin_in"), 16)
                pe.wait_ge(sem("silu"), 1)
                for l in range(2):
                    s = silu[:, l * B:(l + 1) * B]
                    for k in range(2):
                        mm((pH, pY)[l][k][0:B, 0:3 * D], s, wmod[l][:, k * 3 * D:(k + 1) * 3 * D])
                    for n in range(6):
                        last = mm(pZ[:, (l * 6 + n) * B:(l * 6 + n + 1) * B], wmod[l][:, n * D:(n + 1) * D], s)
                last.then_inc(sem("mod_ready"), 1)
                pe.wait_ge(sem("consts"), 1)
                for _, step in steps[0]:
                    step((0, 0), None)
                pe.wait_ge(sem("mod_read"), 1)
                pe.wait_ge(sem("spread_made"), 1)
                pe.wait_ge(sem("b2_lo"), 1)

            whole_program(pe, attention, slot, steps, post, nothing)

        @block.scalar
        def _(act):
            def slot(f, q, prev):
                if not f:
                    return
                act.wait_ge(sem("hid_ready"), chunks(f, q + 1))
                s, k = low_part(f, q)
                act.wait_ge(s, k)
                nc.scalar.activation(g32[:, q % GRING, :], pH[q % 2][:, :], ACT.Gelu, bias=b1(f, q),
                                     scale=1.0 / WSCALE).then_inc(sem("gelu_done"), 1)
                if q == 2:
                    act.wait_ge(sem("gap"), nth(f))
                    nc.scalar.activation(th[:, :], gap[:, :], ACT.Tanh, scale=0.5).then_inc(sem("th"), 1)
                if q == 6:
                    act.wait_ge(sem("cw_turned"), nth(f))
                    nc.scalar.activation(cwT[:, :], pC16, ACT.Copy).then_inc(sem("cwT"), 1)
                e = {7: 0, 8: 1}.get(q, (q - 3) // FC if q >= 11 and q % FC == 3 else None)
                if e is not None and e < NE:
                    act.wait_ge(sem("cwb_ready"), over((NE, NE), f, e + 1))
                    act.wait_ge(sem("y_used"), experts(f, e + 1))
                    nc.scalar.activation(cwb[:, e % 2, :], pC[:, :], ACT.Copy).then_inc(sem("cwb_done"), 1)

            def turned_hn(a, f):
                if f is None:
                    act.wait_ge(sem("vecs_in"), 16)
                act.wait_ge(sem("hn_turned"), nth(a))
                nc.scalar.activation(hnT[:, :], pA[0][:, :], ACT.Identity, bias=beta, scale=gamma).then_inc(sem("hnT"), 1)

            def exp_keys(a, f):
                act.wait_ge(sem("negmax"), nth(a))
                for b in range(GB):
                    last = nc.scalar.activation(bt(eT, b), bt(pA[1], b), ACT.Exp, bias=negmax[:, b:b + 1],
                                                accum_out=esum[:, b:b + 1])
                last.then_inc(sem("exp_done"), 1)

            def copy_v(a, f):
                if a[0]:
                    act.wait_ge(sem("sum_ready"), a[1] * 3 + 3)
                else:
                    act.wait_ge(sem("v_ready"), nth(a))
                nc.scalar.activation(v_tok[:, :], pA[0][:, :], ACT.Copy).then_inc(sem("v_tok"), 1)

            def copy_e(a, f):
                act.wait_ge(sem("e_turned"), nth(a))
                nc.scalar.activation(e_tok[:, :], pA[1][:, :], ACT.Copy).then_inc(sem("e_tok"), 1)

            def modulate(kind_scale, kind_shift, src, dst, name, turned):
                def step(a, f):
                    act.wait_ge(sem(turned), nth(a))
                    if f is not None and name == "hT":
                        act.wait_ge(sem("acc_init"), nth(f))
                    if f is None:
                        act.wait_ge(sem("cols_made"), 1)
                    for j in range(GB):
                        last = nc.scalar.activation(bt(dst, j), bt(src, j), ACT.Identity,
                                                    bias=col(a, kind_shift, j), scale=col(a, kind_scale, j))
                    last.then_inc(sem(name), 1)
                return step

            def low_bands(n):
                def step(a, f):
                    act.wait_ge(sem("bands_ready"), a[1] * 3 + n + 1)
                    nc.scalar.activation(low[:, 0, :], pA[0][:, :], ACT.Copy)
                    nc.scalar.activation(low[:, 1, :], pA[1][:, :], ACT.Copy).then_inc(sem("bands"), 1)
                return step

            def exp_scores(a, f):
                act.wait_ge(sem("negmax"), nth(a))
                for t in range(TT):
                    b, j = divmod(t, TT // GB)
                    last = nc.scalar.activation(prob[:, t, :], bt(pA[b], j), ACT.Exp, bias=negmax[:, t:t + 1],
                                                accum_out=esum[:, t:t + 1])
                last.then_inc(sem("exp_done"), 1)

            def copy_prob(a, f):
                act.wait_ge(sem("prob_turned"), a[1] + 1)
                nc.scalar.activation(probT[:, 0, :, :].rearrange("p k n -> p (k n)"), pA[0][:, :],
                                     ACT.Copy).then_inc(sem("probT_s"), 1)

            def copy_mix(a, f):
                act.wait_ge(sem("mix_ready"), a[1] + 1)
                nc.scalar.activation(yT[:, :], pA[0][:, :], ACT.Copy).then_inc(sem("yT"), 1)

            def split_w(layer, e, n, i=0):
                place = n % STG
                act.wait_ge(sem(f"w_in{place}"), i * 16 + 16 * (n // STG + 1))
                nc.scalar.activation(w_hi[layer][:, at(e), :, :].rearrange("p e k n -> p (e k n)"),
                                     w_stage[:, place, :, :].rearrange("p k n -> p (k n)"), ACT.Copy,
                                     scale=WSCALE).then_inc(sem("w_hi_done"), 1)

            def split_w1(j):
                def step(a, f):
                    if a[0] == 0:
                        if f is not None:
                            split_w(1, f[1] * PER_LOOP + j, NE + j, f[1])
                return step

            def split_last(a, f):
                split_w(1, EXPERTS[1] - 1, sum(EXPERTS) - 1)

            modulate_x2 = modulate(4, 3, pA[0], hT, "hT", "xn2_turned")
            steps = [
                [(6, split_w1(0)), (9, turned_hn), (12, exp_keys), (12, copy_v), (13, copy_e), (16, split_w1(1)),
                 (24, split_w1(2)), (27, modulate_x2)],
                [(7, modulate(1, 0, pA[0], hnT, "hnT", "hn_turned")), (8, low_bands(0)), (10, low_bands(1)),
                 (12, low_bands(2)), (13, copy_v), (16, exp_scores), (17, copy_prob), (19, copy_mix),
                 (27, modulate_x2)]]

            def attention():
                act.wait_ge(sem("modin_in"), 16)
                nc.scalar.activation(sig[:, :], modin[:, 0:2 * B], ACT.Exp, scale=-1.0).then_inc(sem("exp_c"), 1)
                for e in range(STG):
                    split_w(0, e, e)
                for _, step in steps[0]:
                    step((0, 0), None)
                    if step is copy_e:
                        split_w(0, STG, STG)
                for e in range(STG + 1, NE):
                    split_w(0, e, e)

            def split_x(a, f):
                if is_last_of_0(f):
                    split_last(a, f)

            whole_program(act, attention, slot, steps, nothing, split_x)

        @block.vector
        def _(dve):
            V = nc.vector

            def plain():
                dve.wait_ge(sem("b2_zero"), 1)

            def slot(f, q, prev):
                if f:
                    dve.wait_ge(sem("gelu_done"), chunks(f, q + 1) + CREDITS["gelu_done"])
                    dve.wait_ge(sem("w2_done"), chunks(f, q + 1))
                    V.tensor_copy(g_hi[:, q % RING, :], g32[:, q % GRING, :]).then_inc(sem("hi_done"), 1)
                    if q % FC not in POOL_CHUNKS:
                        dve.wait_ge(sem("hi_done"), chunks(f, q + 1))
                        V.tensor_tensor(g_lo[:, q % RING, :], g32[:, q % GRING, :], g_hi[:, q % RING, :],
                                        ALU.subtract).then_inc(low_part(f, q)[0], 1)
                    if q == 1:
                        route_top(f)
                    if q == 4:
                        route_weights(f)
                    if q == 8:
                        dve.wait_ge(sem("b2_term"), nth(f))
                        dve.wait_ge(sem("z_turned"), nth(f, 0) + FIRST)
                        if f[0]:
                            V.tensor_scalar(acc[:, :], pZ[:, :], sb2[:, 0:1], None, ALU.add).then_inc(sem("acc_init"), 1)
                        else:
                            V.tensor_tensor(acc[:, :], pZ[:, :], hT[:, :], ALU.add).then_inc(sem("acc_init"), 1)
                done = expert_at(f, q, prev, 8 if q == 8 and f else 6)
                if q == 6:
                    done = None
                if done:
                    g, e = done
                    dve.wait_ge(sem("w2_done"), chunks(g, FC * (e + 1)) + CREDITS["w2_done"])
                    dve.wait_ge(sem("add_done"), experts(g, e + 1))
                    if e < NE:
                        dve.wait_ge(sem("cwb_done"), over((NE, NE), g, e + 1) + FIRST)
                        V.tensor_tensor(yw[:, e % 2, :], pY[e % 2][:, :], cwb[:, e % 2, :],
                                        ALU.mult).then_inc(sem("y_used"), 1)
                    else:
                        V.tensor_scalar(yw[:, e % 2, :], pY[e % 2][:, :], 1.0 / (NSH * WSCALE), None,
                                        ALU.mult).then_inc(sem("y_used"), 1)

            def route_top(f):
                dve.wait_ge(sem("logits"), nth(f))
                V.tensor_tensor(lg[:, :, :], pC[:, 0:TT * NE].rearrange("p (t e) -> p t e", e=NE),
                                br[f[0]].unsqueeze(1).broadcast_to([P, TT, NE]), ALU.add).then_inc(sem("lg"), 1)
                plain()
                dve.wait_ge(sem("lg"), nth(f))
                for t in range(TT):
                    last = V.max(top[:, t, :], lg[:, t, :])
                last.then_inc(sem("top"), 1)
                dve.wait_ge(sem("top"), nth(f))
                V.tensor_tensor(gap[:, :], top[:, :, 0], top[:, :, 1], ALU.subtract).then_inc(sem("gap"), 1)
                for t in range(TT):
                    last = V.max_index(topi[:, t, :], top[:, t, :], lg[:, t, :])
                last.then_inc(sem("topi"), 1)

            def route_weights(f):
                dve.wait_ge(sem("th"), nth(f))
                dve.wait_ge(sem("topi"), nth(f))
                V.tensor_scalar(pr[:, 0, :], th[:, :], 0.5, 0.5, ALU.mult, ALU.add)
                V.tensor_scalar(pr[:, 1, :], th[:, :], -0.5, 0.5, ALU.mult, ALU.add)
                V.tensor_copy(topf[:, :, :], topi[:, :, :]).then_inc(sem("topf"), 1)
                dve.wait_ge(sem("topf"), nth(f))
                for k in range(2):
                    for t in range(TT):
                        last = V.tensor_scalar(pick[:, k, t, :], iota8[:, :], topf[:, t, k:k + 1], pr[:, k, t:t + 1],
                                               ALU.is_equal, ALU.mult)
                last.then_inc(sem("pick"), 1)
                dve.wait_ge(sem("pick"), nth(f))
                V.tensor_tensor(cw[:, :, :], pick[:, 0, :, :], pick[:, 1, :, :], ALU.add).then_inc(sem("cw"), 1)
                dve.wait_ge(sem("cw"), nth(f))
                V.tensor_copy(cw_parts[:, :, 0:NE], cw[:, :, :]).then_inc(sem("cw_hi"), 1)
                dve.wait_ge(sem("cw_hi"), nth(f))
                V.tensor_tensor(cw_parts[:, :, NE:2 * NE], cw[:, :, :], cw_parts[:, :, 0:NE],
                                ALU.subtract).then_inc(sem("cw_parts"), 1)

            def stats(src, six, two, n, name):
                for t in range(TT):
                    last = V.bn_stats(six[:, t, :], src(t))
                last.then_inc(sem(name + "_six"), 1)
                dve.wait_ge(sem(name + "_six"), n)
                V.memset(carrier[:, :], 0.0)
                for t in range(TT):
                    last = V.bn_aggr(two[:, t, :], six[:, t, :])
                last.then_inc(sem(name + "_mv"), 1)

            def post(f, q):
                if f[0] == 0 and q == 3:
                    plain()
                    dve.wait_ge(sem("z_turned"), nth(f) + FIRST)
                    stats(lambda t: tc(pZ, t), zst6, zmv, nth(f), "z")
                if f[0] == 0 and q == 4:
                    dve.wait_ge(sem("z_rstd"), f[1] + 1)
                    for t in range(TT):
                        last = V.tensor_scalar(zn[:, t, :], tc(pZ, t), zmv[:, t, 0:1], zrstd[:, t:t + 1],
                                               ALU.subtract, ALU.mult)
                    last.then_inc(sem("z_read"), 1)
                if f[0] == 1 and q == 3:
                    dve.wait_ge(sem("add_done"), experts(f, EXPERTS[1]) + CREDITS["add_done"])
                    for j in range(GB):
                        last = V.tensor_scalar(bt(acc, j), bt(acc, j), col(f, 5, j), None, ALU.mult)
                    last.then_inc(sem("acc_gated"), 1)
                if f[0] == 1 and q == 4:
                    dve.wait_ge(sem("z_turned"), nth(f) + FIRST)
                    V.tensor_tensor(xg(f), pZ[:, :].rearrange("p (t d) -> p t d", d=D), xg(f),
                                    ALU.add).then_inc(sem("z_read"), 1)

            def x_stats(a, f):
                plain()
                if a[0]:
                    dve.wait_ge(sem("x_ffn"), a[1] + 1)
                else:
                    dve.wait_ge(sem("x_in0"), 16)
                    if f is not None:
                        dve.wait_ge(sem("x_in1"), 16)
                stats(lambda t: xt(a, t), st6, mv, nth(a), "x")

            def modulate_tok(a, f):
                dve.wait_ge(sem("x_rstd"), nth(a))
                dve.wait_ge(sem("rows_in0"), 16)
                if f is not None:
                    dve.wait_ge(sem("rows_in1"), 16 * (G - 1))
                for t in range(TT):
                    last = V.scalar_tensor_tensor(out=h_tok[:, t:t + 1, :], in0=xt(a, t), scalar=mv[:, t, 0:1],
                                                  in1=row(a, "ca1", t), op0=ALU.subtract, op1=ALU.mult)
                last.then_inc(sem("h_scaled"), 1)
                dve.wait_ge(sem("h_scaled"), nth(a))
                for t in range(TT):
                    last = V.scalar_tensor_tensor(out=h_tok[:, t:t + 1, :], in0=h_tok[:, t:t + 1, :],
                                                  scalar=rstd[:, t:t + 1], in1=row(a, "sa", t),
                                                  op0=ALU.mult, op1=ALU.add)
                last.then_inc(sem("h_tok"), 1)

            def h_stats(a, f):
                plain()
                dve.wait_ge(sem("h_tok"), nth(a))
                stats(lambda t: h_tok[:, t, :], st6, mv, nth(a), "h")

            def normalise(src, rst, name):
                def step(a, f):
                    dve.wait_ge(sem(rst), nth(a))
                    for t in range(TT):
                        last = V.tensor_scalar(hn[:, t:t + 1, :], src(a, t), mv[:, t, 0:1], rstd[:, t:t + 1],
                                               ALU.subtract, ALU.mult)
                    last.then_inc(sem(name), 1)
                return step

            def key_max(a, f):
                dve.wait_ge(sem("k_ready"), nth(a))
                V.tensor_reduce(negmax[:, 0:GB], pA[1][:, :].rearrange("p (b n) -> p b n", b=GB), AX_X, ALU.max,
                                negate=True).then_inc(sem("negmax"), 1)

            def key_sums(a, f):
                dve.wait_ge(sem("exp_done"), nth(a))
                V.reciprocal(rsum[:, 0:GB], esum[:, 0:GB]).then_inc(sem("rsum"), 1)
                dve.wait_ge(sem("rsum"), nth(a))
                V.tensor_scalar(rsum_s[:, 0:GB], rsum[:, 0:GB], float(DH) ** -0.5, None,
                                ALU.mult).then_inc(sem("rsum_s"), 1)

            def mask_context(a, f):
                dve.wait_ge(sem("ctx_ready"), nth(a))
                V.tensor_tensor(ctxm[:, :, :], pA[0][:, 0:GB * D].rearrange("p (b d) -> p b d", d=D),
                                heads[:, :].unsqueeze(1).broadcast_to([P, GB, D]), ALU.mult).then_inc(sem("ctxm"), 1)

            def scale_context(a, f):
                dve.wait_ge(sem("ctxw_ready"), nth(a))
                dve.wait_ge(sem("rsum_s"), nth(a))
                for b in range(GB):
                    last = V.tensor_scalar(ctxw[:, b, :], tc(pA[1], b), rsum_s[:, b:b + 1], None, ALU.mult)
                last.then_inc(sem("ctxw"), 1)

            def copy_qctx(a, f):
                dve.wait_ge(sem("qctx_ready"), nth(a))
                V.tensor_copy(qctx[:, :, :], pA[0][:, 0:GB * D].rearrange("p (b d) -> p b d", d=D)).then_inc(sem("qctx"), 1)

            def add_h(a, f):
                dve.wait_ge(sem("proj_ready"), nth(a))
                V.tensor_tensor(att[:, :, :], pA[1][:, :].rearrange("p (t d) -> p t d", d=D), h_tok[:, :, :],
                                ALU.add).then_inc(sem("att"), 1)

            def x2_stats(a, f):
                plain()
                dve.wait_ge(sem("x_att"), nth(a))
                stats(lambda t: xt(a, t), st6, mv, nth(a), "x2")

            def split_x(a, f):
                dve.wait_ge(sem("hT"), nth(a) + FIRST)
                if f is not None:
                    dve.wait_ge(sem("hid_ready"), chunks(f, FC * EXPERTS[f[0]]))
                V.tensor_copy(x_hi[:, :], hT[:, :]).then_inc(sem("x_hi"), 1)
                dve.wait_ge(sem("x_hi"), nth(a))
                V.tensor_tensor(x_lo[:, :], hT[:, :], x_hi[:, :], ALU.subtract).then_inc(sem("x_split"), 1)
                if is_last_of_0(f):
                    split_w(1, EXPERTS[1] - 1, sum(EXPERTS) - 1)

            def cast_h(a, f):
                dve.wait_ge(sem("hnT"), nth(a))
                V.tensor_copy(h16[:, :], hnT[:, :]).then_inc(sem("h16"), 1)

            def copy_q(a, f):
                dve.wait_ge(sem("sum_ready"), a[1] * 3 + 1)
                V.tensor_scalar(qT[:, :], pA[0][:, :], float(D) ** -0.5, None, ALU.mult).then_inc(sem("q_done"), 1)

            def copy_k(a, f):
                dve.wait_ge(sem("sum_ready"), a[1] * 3 + 2)
                V.tensor_copy(kT[:, :], pA[0][:, :]).then_inc(sem("k_done"), 1)

            def score_max(a, f):
                dve.wait_ge(sem("scores"), a[1] + 1)
                for b in range(GB):
                    last = V.tensor_reduce(negmax[:, 2 * b:2 * b + 2], pA[b][:, :].rearrange("p (j n) -> p j n", j=2),
                                           AX_X, ALU.max, negate=True)
                last.then_inc(sem("negmax"), 1)

            def score_sums(a, f):
                dve.wait_ge(sem("exp_done"), nth(a))
                V.reciprocal(rsum[:, :], esum[:, :]).then_inc(sem("rsum"), 1)

            def copy_prob(a, f):
                dve.wait_ge(sem("prob_turned"), a[1] + 1)
                V.tensor_copy(probT[:, 1, :, :].rearrange("p k n -> p (k n)"), pA[1][:, :]).then_inc(sem("probT_v"), 1)

            def gate_att(a, f):
                dve.wait_ge(sem("proj_ready"), nth(a))
                dve.wait_ge(sem("rsum"), nth(a))
                for t in range(TT):
                    last = V.scalar_tensor_tensor(out=att[:, t:t + 1, :], in0=tc(pA[1], t).unsqueeze(1), scalar=rsum[:, t:t + 1],
                                                  in1=row(a, "ga_1", t), op0=ALU.mult, op1=ALU.mult)
                last.then_inc(sem("att"), 1)

            def split_w(layer, e, n, i=0):
                place = n % STG
                dve.wait_ge(sem("w_hi_done"), i * STG + (n + 1))
                V.scalar_tensor_tensor(out=w_lo[layer][:, at(e), :, :].rearrange("p e k n -> p (e k n)"),
                                       in0=w_stage[:, place, :, :].rearrange("p k n -> p (k n)"), scalar=WSCALE,
                                       in1=w_hi[layer][:, at(e), :, :].rearrange("p e k n -> p (e k n)"),
                                       op0=ALU.mult, op1=ALU.subtract).then_inc(sem("w_lo_done"), 1)

            def split_w1(j):
                def step(a, f):
                    if f is not None and a[0] == 0:
                        split_w(1, f[1] * PER_LOOP + j, NE + j, f[1])
                return step

            steps = [
                [(5, x_stats), (6, modulate_tok), (7, h_stats), (8, normalise(lambda a, t: h_tok[:, t:t + 1, :], "h_rstd", "hn")),
                 (9, split_w1(0)), (11, key_max), (12, key_sums), (15, mask_context), (17, scale_context), (19, copy_qctx),
                 (19, split_w1(1)), (21, add_h), (24, x2_stats), (25, normalise(xt, "x2_rstd", "xn2")), (27, split_w1(2))],
                [(5, x_stats), (6, normalise(xt, "x_rstd", "hn")), (7, cast_h), (9, copy_q), (11, copy_k), (15, score_max),
                 (16, score_sums), (17, copy_prob), (21, gate_att), (24, x2_stats), (25, normalise(xt, "x2_rstd", "xn2"))]]

            def attention():
                chain = [0]

                def link(ins):
                    chain[0] += 1
                    ins.then_inc(sem("setup"), 1)
                    dve.wait_ge(sem("setup"), chain[0])

                dve.wait_ge(sem("exp_c"), 1)
                link(V.tensor_scalar(sig[:, :], sig[:, :], 1.0, None, ALU.add))
                link(V.reciprocal(sig[:, :], sig[:, :]))
                V.tensor_tensor(silu[:, :], sig[:, :], modin[:, 0:2 * B], ALU.mult).then_inc(sem("silu"), 1)
                dve.wait_ge(sem("mod_ready"), 1)
                for l in range(2):
                    for k in range(2):
                        last = V.tensor_copy(modr[:, l, 3 * k:3 * k + 3, :].rearrange("b k d -> b (k d)"),
                                             (pH, pY)[l][k][0:B, 0:3 * D])
                link(last)
                link(V.tensor_copy(cols[:, :, :, :].rearrange("p l k b -> p (l k b)"), pZ[:, 0:12 * B]))
                gates = [modr[:, 0, 2, :], modr[:, 0, 5, :], modr[:, 1, 2, :]]
                for n, g in enumerate(gates):
                    V.tensor_scalar(signr[:, n, :], g, 0.0, 2.0, ALU.is_ge, ALU.mult)
                    last = V.tensor_scalar(magr[:, n, :], g, -1.0, None, ALU.mult)
                link(last)
                for n, g in enumerate(gates):
                    last = V.scalar_tensor_tensor(out=magr[:, n, :], in0=g, scalar=0.25, in1=magr[:, n, :],
                                                  op0=ALU.max, op1=ALU.max)
                link(last)
                link(V.scalar_tensor_tensor(out=signr[:, :, :], in0=signr[:, :, :], scalar=1.0, in1=magr[:, :, :],
                                            op0=ALU.subtract, op1=ALU.mult))
                dve.wait_ge(sem("bvec_in"), 16)
                b_out, ln_w, ln_b, out_b = (bvec[0:B, n * D:(n + 1) * D] for n in range(4))
                V.tensor_scalar(rowc[:, 0, :], modr[:, 0, 1, :], 1.0, None, ALU.add)
                V.tensor_copy(rowc[:, 1, :], modr[:, 0, 0, :])
                V.tensor_copy(rowc[:, 2, :], signr[:, 0, :])
                V.tensor_tensor(rowc[:, 3, :], signr[:, 0, :], b_out, ALU.mult)
                V.tensor_tensor(rowc[:, 4, :], signr[:, 1, :], ln_w, ALU.mult)
                V.tensor_tensor(rowc[:, 5, :], signr[:, 1, :], ln_b, ALU.mult)
                V.tensor_copy(rowc[:, 6, :], signr[:, 2, :])
                V.tensor_tensor(rowc[:, 7, :], signr[:, 2, :], out_b, ALU.mult).then_inc(sem("rows_made"), 1)
                for l in range(2):
                    for k in (1, 4):
                        V.tensor_scalar(cols[:, l, k, :], cols[:, l, k, :], 1.0, None, ALU.add)
                V.tensor_scalar(signc[:, :], cols[:, 1, 5, :], 0.0, 2.0, ALU.is_ge, ALU.mult)
                link(V.tensor_scalar(sig[:, 0:B], cols[:, 1, 5, :], -1.0, None, ALU.mult))
                link(V.scalar_tensor_tensor(out=sig[:, B:2 * B], in0=cols[:, 1, 5, :], scalar=0.25, in1=sig[:, 0:B],
                                            op0=ALU.max, op1=ALU.max))
                V.scalar_tensor_tensor(out=cols[:, 1, 5, :], in0=signc[:, :], scalar=1.0, in1=sig[:, B:2 * B],
                                       op0=ALU.subtract, op1=ALU.mult).then_inc(sem("cols_made"), 1)
                dve.wait_ge(sem("cols_made"), 1)
                V.memset(cw_parts[:, :, :], 0.0).then_inc(sem("mod_read"), 1)
                dve.wait_ge(sem("mod_read"), 1)
                dve.wait_ge(sem("b2_in"), 32)
                dve.wait_ge(sem("vecs_in"), 16)
                link(V.tensor_copy(b2_hi[:, :, :], b2[:, :, :]))
                V.tensor_tensor(b2_lo[:, :, :], b2[:, :, :], b2_hi[:, :, :], ALU.subtract).then_inc(sem("b2_lo"), 1)
                link(V.tensor_tensor(sb2[:, 1:2], vecs[:, 2:3], vecs[:, 3:4], ALU.add))
                link(V.tensor_scalar(sb2[:, 0:1], sb2[:, 1:2], 1.0 / NSH, None, ALU.mult))
                dve.wait_ge(sem("consts"), 1)
                e = 0
                for _, step in steps[0]:
                    step((0, 0), None)
                    if step in (key_max, mask_context, scale_context):
                        split_w(0, e, e)
                        e += 1
                for e in range(e, NE):
                    split_w(0, e, e)

            whole_program(dve, attention, slot, steps, post, split_x)

        @block.gpsimd
        def _(pool):
            O = nc.gpsimd

            def plain(value=0):
                pool.compute_val(value)
                pool.wait_ge(sem("neghalf"), 1)

            def slot(f, q, prev):
                if f and q % FC in POOL_CHUNKS:
                    pool.wait_ge(sem("hi_done"), chunks(f, q + 1))
                    O.tensor_tensor(g_lo[:, q % RING, :], g32[:, q % GRING, :], g_hi[:, q % RING, :],
                                    ALU.subtract).then_inc(low_part(f, q)[0], 1)
                done = expert_at(f, q, prev, 8 if q == 8 and f else 6)
                if q == 6:
                    done = None
                if done:
                    g, e = done
                    pool.wait_ge(sem("y_used"), experts(g, e + 1) + CREDITS["y_used"])
                    if e == 0:
                        pool.wait_ge(sem("acc_init"), nth(g))
                    else:
                        pool.wait_ge(sem("add_done"), experts(g, e) + CREDITS["add_done"])
                    O.tensor_tensor(acc[:, :], acc[:, :], yw[:, e % 2, :], ALU.add).then_inc(sem("add_done"), 1)

            def power(src, which, n, dst, tmp, name):
                pool.wait_ge(sem(name + "_mv"), n)
                O.tensor_tensor(tmp[:, :], src[:, :, 1], eps[:, which, :], ALU.add).then_inc(sem(name + "_veps"), 1)
                pool.wait_ge(sem(name + "_veps"), n)
                O.tensor_tensor(dst[:, :], tmp[:, :], neghalf[:, :], ALU.pow).then_inc(sem(name + "_rstd"), 1)

            def post(f, q):
                if f[0] == 0 and q == 3:
                    power(zmv, 1, nth(f), zrstd, zveps, "z")
                if f[0] == 0 and q == 4:
                    plain(nth(f) + FIRST)
                    pool.wait_ge(sem("z_read"), nth(f) + FIRST)
                    O.tensor_tensor(by_batch(zn[:, :, :]), by_batch(zn[:, :, :]), rowg(f, "gblw"), ALU.mult).then_inc(sem("zn_w"), 1)
                    plain()
                    pool.wait_ge(sem("zn_w"), f[1] + 1)
                    O.tensor_tensor(by_batch(zn[:, :, :]), by_batch(zn[:, :, :]), rowg(f, "gblb"), ALU.add).then_inc(sem("zn_b"), 1)
                    plain()
                    pool.wait_ge(sem("zn_b"), f[1] + 1)
                    O.tensor_tensor(xg(f), xg(f), zn[:, :, :], ALU.add).then_inc(sem("x_ffn"), 1)

            def rstd_of(name):
                def step(a, f):
                    power(mv, 0, nth(a), rstd, veps, name)
                return step

            def add_bias(name, read):
                def step(a, f):
                    plain()
                    pool.wait_ge(sem(read), nth(a))
                    if f is None:
                        pool.wait_ge(sem("rows_in0"), 16)
                    elif a[0] == 0:
                        pool.wait_ge(sem("rows_in1"), 16 * (G - 1))
                    O.tensor_tensor(by_batch(xg(a)), by_batch(xg(a)), rowg(a, name), ALU.add).then_inc(sem("x_bias"), 1)
                return step

            def add_att0(a, f):
                plain(nth(a) + FIRST)
                pool.wait_ge(sem("att"), nth(a) + FIRST)
                O.tensor_tensor(by_batch(att[:, :, :]), by_batch(att[:, :, :]), rowg(a, "ga"), ALU.mult).then_inc(sem("att_g"), 1)
                plain()
                pool.wait_ge(sem("att_g"), nth(a))
                pool.wait_ge(sem("x_bias"), nth(a))
                O.tensor_tensor(xg(a), xg(a), att[:, :, :], ALU.add).then_inc(sem("x_att"), 1)

            def add_att1(a, f):
                plain(nth(a) + FIRST)
                pool.wait_ge(sem("att"), nth(a) + FIRST)
                pool.wait_ge(sem("x_bias"), nth(a))
                O.tensor_tensor(xg(a), xg(a), att[:, :, :], ALU.add).then_inc(sem("x_att"), 1)

            steps = [
                [(5, rstd_of("x")), (7, rstd_of("h")), (8, add_bias("gab", "h_tok")), (21, add_att0), (24, rstd_of("x2"))],
                [(5, rstd_of("x")), (8, add_bias("gab_1", "hn")), (21, add_att1), (24, rstd_of("x2"))]]

            def attention():
                for name, n in CREDITS.items():
                    pool.sem_inc(sem(name), n)
                done = [0]

                def link(ins):
                    done[0] += 1
                    ins.then_inc(sem("pool_setup"), 1)
                    pool.wait_ge(sem("pool_setup"), done[0])

                O.memset(b2[:, :, :], 0.0).then_inc(sem("b2_zero"), 1)
                pool.wait_ge(sem("b2_zero"), 1)
                link(O.memset(eps[:, 0, :], LN_EPS))
                link(O.memset(eps[:, 1, :], LN_EPS_FFN))
                O.memset(neghalf[:, :], -0.5).then_inc(sem("neghalf"), 1)
                pool.wait_ge(sem("neghalf"), 1)
                link(O.memset(ident[:, :], 0.0))
                link(O.affine_select(out=ident[:, :], in_=ident[:, :], compare_op=ALU.not_equal, fill=1.0, base=0,
                                     pattern=[[-1, P]], channel_multiplier=1))
                link(O.memset(heads[:, :], 0.0))
                for h in range(D // DH):
                    s = slice(h * DH, (h + 1) * DH)
                    link(O.memset(heads[s, s], 1.0))
                link(O.iota(iota8[:, :], [[1, NE]], base=0, channel_multiplier=0,
                            allow_small_or_imprecise_dtypes=True))
                O.tensor_copy(ident16[:, :], ident[:, :]).then_inc(sem("consts"), 1)
                pool.wait_ge(sem("consts"), 1)
                link(O.memset(spread[:, :, :], 0.0))
                for k in range(2):
                    link(O.affine_select(out=spread[:, :, :], in_=spread[:, :, :], compare_op=ALU.not_equal,
                                         fill=1.0 / WSCALE, base=-k * NE, pattern=[[-1, NE], [0, P]],
                                         channel_multiplier=1))
                link(O.memset(wmid[:, :], 0.0))
                O.memset(wband[:, :, :], 0.0).then_inc(sem("spread_made"), 1)
                pool.wait_ge(sem("spread_made"), 1)
                for _, step in steps[0]:
                    step((0, 0), None)
                pool.wait_ge(sem("att1_in"), 16)
                for k in range(2):
                    rows_k = slice(k * (P - BAND), k * (P - BAND) + BAND)
                    link(O.tensor_copy(wband[rows_k, k, :], att1[rows_k, 0:3 * D]))
                for k in (1, 2):
                    rows_k = slice(k * BAND, (k + 1) * BAND)
                    last = O.tensor_copy(wmid[rows_k, :], att1[rows_k, 0:3 * D])
                    if k == 1:
                        link(last)
                last.then_inc(sem("bands_made"), 1)
                pool.wait_ge(sem("bands_made"), 1)

            whole_program(pool, attention, slot, steps, post, nothing)


INPUTS = ("modin", "x", "bvec", "vecs", "att0", "att1", "b2", "w_0", "w_1")


def kernel(**inputs):
    import numpy as np
    import concourse.bacc as bacc
    from concourse.bass_utils import run_bass_kernel_spmd

    v = {k: np.asarray(a) for k, a in inputs.items()}
    l0 = {k[3:]: a for k, a in v.items() if k.startswith("L0_")}
    l1 = {k[3:]: a for k, a in v.items() if k.startswith("L1_")}

    def by_chunk(b):
        return b.reshape(-1, FC, P).transpose(2, 0, 1).reshape(P, -1)

    def w1_w2(w1, w2):
        w2 = w2.reshape(-1, FC, P, D).transpose(0, 2, 1, 3).reshape(-1, P, F)
        return np.stack([w1, w2], axis=2)

    w_qkv = l0["attn_w_qkv"]
    arrays = {
        "x": l0["attn_x"].reshape(-1, P, D).transpose(1, 0, 2),
        "modin": np.concatenate([l0["c"].T, l1["c"].T, l0["wmod"], l1["wmod"]], axis=1),
        "bvec": np.concatenate([l0["attn_b_out"], l0["ffn_ln_w"], l0["ffn_ln_b"], l1["attn_out_b"],
                                l0["ffn_br"], l1["ffn_rb"]]),
        "vecs": np.concatenate([l0["attn_gamma"].reshape(D, 1), l0["attn_beta"].reshape(D, 1), l1["ffn_sb2"].T,
                                by_chunk(l0["ffn_b1"]), by_chunk(l1["ffn_b1"]), by_chunk(l1["ffn_sb1"])], axis=1),
        "att0": np.concatenate([w_qkv[:, D:2 * D], w_qkv[:, 2 * D:], l0["attn_w_out"], w_qkv[:, :D].T,
                                l0["ffn_Wr"].T, l1["ffn_rW"]], axis=1),
        "att1": np.concatenate([l1["attn_weight_qkv"], l1["attn_out_w"].T], axis=1),
        "b2": np.stack([l0["ffn_b2"], l1["ffn_b2"]], axis=1),
        "w_0": w1_w2(l0["ffn_W1"].transpose(0, 2, 1), l0["ffn_W2"].transpose(0, 2, 1)),
        "w_1": w1_w2(np.concatenate([l1["ffn_W1"], l1["ffn_sW1"]]), np.concatenate([l1["ffn_W2"], l1["ffn_sW2"]])),
    }
    arrays = {f"in_{n}": np.ascontiguousarray(arrays[n]) for n in INPUTS}
    nc = bacc.Bacc("TRN2", target_bir_lowering=False, num_devices=1)
    dram = {n: nc.dram_tensor(f"in_{n}", arrays[f"in_{n}"].shape, F32, kind="ExternalInput").ap() for n in INPUTS}
    out = nc.dram_tensor("out", (P, B * N // P, D), F32, kind="ExternalOutput").ap()
    build(nc, dram, out)
    r = run_bass_kernel_spmd(nc, [arrays], core_ids=[0])
    return r.results[0]["out"].transpose(1, 0, 2).reshape(B, N, D)
```
